# Optimizing a Trainium2 kernel written in Bass

```python
import numpy as np
import jax
import jax.numpy as jnp

def _softmax(x, axis=-1):
    return jax.nn.softmax(x, axis=axis)
def _gelu(x):
    return jax.nn.gelu(x, approximate=True)
def _silu(x):
    return jax.nn.silu(x)
def _sigmoid(x):
    return jax.nn.sigmoid(x)
def _layernorm(x, axis=-1, eps=1e-5):
    m = jnp.mean(x, axis=axis, keepdims=True)
    v = jnp.var(x, axis=axis, keepdims=True)
    return (x - m) / jnp.sqrt(v + eps)
def _scatter_add(tgt, idx, src, axis=0):
    return tgt.at[idx].add(src)
def _segment_sum(src, seg, n):
    return jax.ops.segment_sum(src, seg, n)

kernel_name = 'mk_conv_seq_d1_conv_nchw64_65ea5e'

def setup_inputs(seed: int = 0):
    np.random.seed(seed)
    _w = jnp.asarray
    def _rec_inputs():
        import jax
        import jax.numpy as jnp
        _gk = jax.random.key(seed)
        x = -3.11e-05 + 0.9999 * jax.random.normal(jax.random.fold_in(_gk, 1), (4, 64, 504, 504), jnp.float32)
        return x
    x = _rec_inputs()
    def _L0_conv_setup():
        import jax, jax.numpy as jnp
        import numpy as np
        LBS = 8
        BS = 4
        IN_CH = 64
        C1 = IN_CH // 4
        OUT_CH = C1 * LBS * LBS

        def pixel_unshuffle(x, r):
            n, c, h, w = x.shape
            x = x.reshape(n, c, h // r, r, w // r, r)
            x = x.transpose(0, 1, 3, 5, 2, 4)
            return x.reshape(n, c * r * r, h // r, w // r)

        def pixel_shuffle(x, r):
            n, c, h, w = x.shape
            x = x.reshape(n, c // (r * r), r, r, h, w)
            x = x.transpose(0, 1, 4, 2, 5, 3)
            return x.reshape(n, c // (r * r), h * r, w * r)
        key = jax.random.key(seed)
        k0, k1, k2, k3, k4 = jax.random.split(key, 5)
        x = jax.random.normal(k0, (4, IN_CH, 504, 504), dtype=jnp.float32)
        w_ptg = jax.random.normal(k1, (3 * C1, IN_CH), dtype=jnp.float32) * 0.05
        b_ptg = jax.random.normal(k2, (3 * C1,), dtype=jnp.float32) * 0.01
        w_out = jax.random.normal(k3, (IN_CH, C1), dtype=jnp.float32) * 0.05
        b_out = jax.random.normal(k4, (IN_CH,), dtype=jnp.float32) * 0.01
        return {'x': x, 'w_ptg': w_ptg, 'b_ptg': b_ptg, 'w_out': w_out, 'b_out': b_out}
    _L0_conv_all = _L0_conv_setup()
    _L0_conv_in = {k: v for k, v in _L0_conv_all.items() if k in ('w_ptg', 'b_ptg', 'w_out', 'b_out', )}
    del _L0_conv_all

    return {
        "x": x,
        "L0_conv_w_ptg": _L0_conv_in["w_ptg"],
        "L0_conv_b_ptg": _L0_conv_in["b_ptg"],
        "L0_conv_w_out": _L0_conv_in["w_out"],
        "L0_conv_b_out": _L0_conv_in["b_out"],
    }

def reference(x, L0_conv_w_ptg, L0_conv_b_ptg, L0_conv_w_out, L0_conv_b_out):
    import jax
    import jax.numpy as jnp
    def _L0_conv_ref(x, w_ptg, b_ptg, w_out, b_out):
        import jax, jax.numpy as jnp
        import numpy as np
        LBS = 8
        BS = 4
        IN_CH = 64
        C1 = IN_CH // 4
        OUT_CH = C1 * LBS * LBS

        def pixel_unshuffle(x, r):
            n, c, h, w = x.shape
            x = x.reshape(n, c, h // r, r, w // r, r)
            x = x.transpose(0, 1, 3, 5, 2, 4)
            return x.reshape(n, c * r * r, h // r, w // r)

        def pixel_shuffle(x, r):
            n, c, h, w = x.shape
            x = x.reshape(n, c // (r * r), r, r, h, w)
            x = x.transpose(0, 1, 4, 2, 5, 3)
            return x.reshape(n, c // (r * r), h * r, w * r)
        y = jnp.einsum('oc,bchw->bohw', w_ptg, x) + b_ptg[None, :, None, None]
        H8, W8 = (y.shape[2], y.shape[3])
        H8div = (H8 // (BS * BS) + 1) * (BS * BS)
        W8div = (W8 // (BS * BS) + 1) * (BS * BS)
        y = jnp.pad(y, ((0, 0), (0, 0), (0, H8div - H8), (0, W8div - W8)))
        y = pixel_unshuffle(y, LBS)
        B, C3, H, W = y.shape
        C = C3 // 3
        yg = pixel_unshuffle(y, BS)
        yb = yg.transpose(0, 2, 3, 1).reshape(-1, C3, BS, BS)
        Nb = yb.shape[0]
        yb = yb.transpose(0, 2, 3, 1).reshape(Nb, BS * BS, C3)
        qn = yb[:, :, :OUT_CH]
        qt = yb[:, :, OUT_CH:2 * OUT_CH]
        g = yb[:, :, 2 * OUT_CH:]
        sa = jax.nn.softmax(jnp.einsum('bik,bjk->bij', qn, qt), axis=2)
        o = jnp.einsum('bij,bjc->bic', sa, g)
        o = o.reshape(Nb, BS, BS, C).transpose(0, 3, 1, 2)
        Hb, Wb = (H // BS, W // BS)
        o = o.reshape(-1, Hb, Wb, C * BS * BS).transpose(0, 3, 1, 2)
        o = pixel_shuffle(o, BS)
        o = pixel_shuffle(o, LBS)
        o = o[:, :, :H8, :W8]
        out = jnp.einsum('oc,bchw->bohw', w_out, o) + b_out[None, :, None, None]
        return out + x

    def _gn(v, G=32, eps=1e-5):
        B_, C_, H_, W_ = v.shape
        g = v.reshape(B_, G, C_ // G, H_, W_)
        m = jnp.mean(g, axis=(2, 3, 4), keepdims=True)
        s = jnp.var(g, axis=(2, 3, 4), keepdims=True)
        return ((g - m) / jnp.sqrt(s + eps)).reshape(v.shape)

    def _ln_c(v, eps=1e-6):
        m = jnp.mean(v, axis=1, keepdims=True)
        s = jnp.var(v, axis=1, keepdims=True)
        return (v - m) / jnp.sqrt(s + eps)

    def _ln_t(v, eps=1e-5):
        m = jnp.mean(v, axis=-1, keepdims=True)
        s = jnp.var(v, axis=-1, keepdims=True)
        return (v - m) / jnp.sqrt(s + eps)

    def _to_tokens(v):
        B_, C_, H_, W_ = v.shape
        return v.reshape(B_, C_, H_ * W_).transpose(0, 2, 1)
    def _from_tokens(t, like):
        B_, C_, H_, W_ = like.shape
        return t.transpose(0, 2, 1).reshape(B_, C_, H_, W_)

    x = _L0_conv_ref(x, L0_conv_w_ptg, L0_conv_b_ptg, L0_conv_w_out, L0_conv_b_out)
    return x


_drawn_inputs = setup_inputs


def setup_inputs(seed=0):
    import zlib

    import numpy as np

    out = dict(_drawn_inputs(seed))
    spreads = {}
    factors = {'L0_conv_b_ptg': 8.0, 'L0_conv_b_out': 5.915}
    for name, (base, spread) in spreads.items():
        noise = np.random.default_rng([zlib.crc32(name.encode()), seed]).standard_normal(out[name].shape)
        drawn = base * np.exp(spread * noise) if base else spread * noise
        out[name] = jnp.asarray(drawn.astype(out[name].dtype))
    for name, factor in factors.items():
        out[name] = (out[name] * factor).astype(out[name].dtype)
    return out
```

```python
import concourse.bass as bass
from concourse import mybir
from contextlib import ExitStack


def block_attention_kernel(nc, x, w_ptg, b_ptg, w_out, b_out, out):
    fp32 = mybir.dt.float32
    fp32r = mybir.dt.float32r
    ALU = mybir.AluOpType
    ACT = mybir.ActivationFunctionType
    AX = mybir.AxisListType

    IMAGES, CH, HEIGHT, WIDTH = x.shape
    C1 = w_out.shape[1]
    PATCH, SIDE = 8, 4
    STRIP = PATCH * SIDE
    HALVES = 2
    ROWS = PATCH // HALVES
    STRIPS = -(-HEIGHT // STRIP)
    SLOTS = 4
    PASSES = IMAGES * STRIPS // SLOTS
    PER_IMAGE = STRIPS // SLOTS
    TOKCOLS = WIDTH // PATCH
    PADCOLS = STRIPS * SIDE
    GROUPS = 2
    GCOLS = PADCOLS // GROUPS
    TOK = SIDE * GCOLS
    KINDS = 3
    RUN = ROWS * WIDTH
    BIG = 1.0e37
    Q, K, G = range(KINDS)
    assert HALVES * CH == 128 and ROWS * HALVES * C1 == 128 and TOK == 128
    assert STRIPS % SLOTS == 0 and WIDTH <= 512

    x_d = x.rearrange("n c h w -> n c (h w)")
    out_d = out.rearrange("n c h w -> n c (h w)")

    ctx = ExitStack()
    with ctx:
        def sb(name, shape, dt=fp32):
            return ctx.enter_context(nc.sbuf_tensor(name, shape, dt))

        def sem(name):
            return ctx.enter_context(nc.semaphore(name))

        X = sb("X", [128, SLOTS, SIDE, ROWS, WIDTH])
        QKG = sb("QKG", [128, KINDS, PATCH, PADCOLS, SIDE])
        GT = sb("GT", [128, GROUPS, PATCH, 128])
        O = sb("O", [128, 2, SIDE, PADCOLS * PATCH], fp32r)
        S = sb("S", [128, GROUPS, TOK])
        E = sb("E", [128, GROUPS, TOK])
        P = sb("P", [128, GROUPS, TOK])
        PT = sb("PT", [128, GROUPS, TOK])
        negmax = sb("negmax", [128, GROUPS])
        rowsum = sb("rowsum", [128, GROUPS])
        inverse = sb("inverse", [128, GROUPS])
        zeros = sb("zeros", [128, PATCH * TOKCOLS])
        ident = sb("ident", [128, 128])
        blocks8 = sb("blocks8", [8, 8, SIDE * SIDE])
        mask = sb("mask", [128, TOK])
        w_nat = sb("w_nat", [KINDS * C1, CH])
        wo_nat = sb("wo_nat", [CH, C1])
        w_st = sb("w_st", [KINDS * C1, HALVES, CH, HALVES])
        wo_st = sb("wo_st", [CH, 2, HALVES, 2, 2, HALVES, C1])
        b_st = sb("b_st", [KINDS + 1, 128])
        W = sb("W", [128, KINDS, HALVES * C1])
        WOH = sb("WOH", [128, 2, CH, HALVES], fp32r)
        WOL = sb("WOL", [128, 2, CH, HALVES], fp32r)
        bias = sb("bias", [128, KINDS + 1])

        PS = ctx.enter_context(nc.psum_tensor("PS", [128, 8, 512], fp32))
        SCORE_BANK = (3, 0)
        WIDE_BANK = (1, 4)
        PT_BANK = (6, 7)
        OUT_BANK = 4

        x_loaded = [[sem(f"x_loaded_{s}_{t}") for t in range(SIDE)] for s in range(SLOTS)]
        out_stored = [[sem(f"out_stored_{s}_{t}") for t in range(SIDE)] for s in range(SLOTS)]
        small_loaded = sem("small_loaded")
        ident_cleared = sem("ident_cleared")
        pads_made = sem("pads_made")
        consts_made = sem("consts_made")
        w_stretched = sem("w_stretched")
        w_turned = sem("w_turned")
        w_high = sem("w_high")
        w_ready = sem("w_ready")
        projected = sem("projected")
        qkg_kept = sem("qkg_kept")
        scored = sem("scored")
        masked = sem("masked")
        maxed = sem("maxed")
        exped = sem("exped")
        inverted = sem("inverted")
        normed = sem("normed")
        p_turned = sem("p_turned")
        p_kept = sem("p_kept")
        g_turned = sem("g_turned")
        g_kept = sem("g_kept")
        mixed = sem("mixed")
        o_high = sem("o_high")
        o_low = sem("o_low")
        out_made = sem("out_made")
        out_kept = sem("out_kept")

        block = ctx.enter_context(nc.Block())

        def dram_rows(t, n, th, may_lack=False):
            row = n % STRIPS
            if may_lack:
                row = row % (STRIPS - 1)
            first = (row * STRIP + th * PATCH) * WIDTH
            return t[n // STRIPS, :, bass.ds(first, HALVES * RUN)]

        def slot_rows(slot, th):
            return X[:, slot, th, :, :].rearrange("p r w -> p (r w)")

        def tokens(kind, col, g):
            return QKG[:, kind, col, g * GCOLS:(g + 1) * GCOLS, :].rearrange("p t s -> p (t s)")

        def o_bank(lanes, b):
            return PS[lanes, b:b + 2, :].rearrange("p b (r t s) -> p (b r) t s", r=PATCH // 2, s=SIDE)

        def o_place(lanes, h, g):
            whole = O[lanes, h, :, :].rearrange("p s (t r) -> p r t s", r=PATCH)
            return whole[:, :, g * GCOLS:(g + 1) * GCOLS, :]

        @block.sync
        def _(sp):
            sp.dma_start(w_nat[:, :], w_ptg).then_inc(small_loaded, 16)
            sp.dma_start(wo_nat[:, :], w_out).then_inc(small_loaded, 16)
            for j in range(ROWS * HALVES):
                sp.dma_start(b_st[0:KINDS, j * C1:(j + 1) * C1],
                             b_ptg.rearrange("(k o) -> k o", k=KINDS)).then_inc(small_loaded, 16)
            with nc.allow_non_contiguous_dma(reason="64 values, once"):
                for a in range(HALVES):
                    sp.dma_start(b_st[KINDS:KINDS + 1, a:128:HALVES],
                                 b_out.rearrange("(k c) -> k c", k=1)).then_inc(small_loaded, 16)

            def load(n, slot, th):
                if slot == SLOTS - 1 and th == SIDE - 1:
                    sp.dma_start(slot_rows(slot, th), dram_rows(x_d, n, th, True),
                                 cond=(n % STRIPS < STRIPS - 1)).then_inc(x_loaded[slot][th], 16)
                else:
                    sp.dma_start(slot_rows(slot, th), dram_rows(x_d, n, th)).then_inc(x_loaded[slot][th], 16)

            def store(n, slot, th):
                if slot == SLOTS - 1 and th == SIDE - 1:
                    sp.dma_start(dram_rows(out_d, n, th, True), slot_rows(slot, th),
                                 cond=(n % STRIPS < STRIPS - 1)).then_inc(out_stored[slot][th], 16)
                else:
                    sp.dma_start(dram_rows(out_d, n, th), slot_rows(slot, th)).then_inc(out_stored[slot][th], 16)

            def strip(i, slot, last):
                n = i * SLOTS + slot
                ahead = (slot + SLOTS - 1) % SLOTS
                for th in range(SIDE):
                    if not last or slot == 0:
                        sp.wait_ge(out_stored[ahead][th], 16 * (i + (2 if slot else 1)))
                        load(n + SLOTS - 1, ahead, th)
                    sp.wait_ge(out_kept, 2 * (SIDE * n + th + 1))
                    if not (last and slot == SLOTS - 1 and th == SIDE - 1):
                        store(n, slot, th)

            for slot in range(SLOTS - 1):
                for th in range(SIDE):
                    load(slot, slot, th)
            for slot in range(SLOTS):
                for th in range(SIDE):
                    sp.sem_inc(out_stored[slot][th], 16)
            with sp.Fori(0, PASSES - 1) as i:
                for slot in range(SLOTS):
                    strip(i, slot, False)
            for slot in range(SLOTS):
                strip(PASSES - 1, slot, True)
            for slot in range(SLOTS):
                for th in range(SIDE):
                    stores = 1 + PASSES - (slot == SLOTS - 1 and th == SIDE - 1)
                    sp.wait_ge(out_stored[slot][th], 16 * stores)

        @block.gpsimd
        def _(pool):
            nc.gpsimd.memset(ident[:, :], 0.0).then_inc(ident_cleared, 1)
            nc.gpsimd.memset(blocks8[:, :, :], 0.0).then_inc(ident_cleared, 1)
            nc.gpsimd.memset(w_st[:, :, :, :], 0.0).then_inc(pads_made, 1)
            nc.gpsimd.memset(wo_st[:, :, :, :, :, :, :], 0.0).then_inc(pads_made, 1)
            pool.wait_ge(ident_cleared, 2)
            nc.gpsimd.affine_select(out=ident[:, :], in_=ident[:, :], compare_op=ALU.not_equal, fill=1.0,
                                    base=0, pattern=[[-1, 128]], channel_multiplier=1).then_inc(consts_made, 1)
            nc.gpsimd.affine_select(out=blocks8[:, :, :], in_=blocks8[:, :, :],
                                    compare_op=ALU.not_equal, fill=1.0, base=0,
                                    pattern=[[-1, 8], [0, SIDE * SIDE]],
                                    channel_multiplier=1).then_inc(consts_made, 1)
            nc.gpsimd.memset(zeros[:, :], 0.0).then_inc(pads_made, 1)
            for kind in range(KINDS):
                nc.gpsimd.memset(QKG[:, kind, :, TOKCOLS:PADCOLS, :], 0.0).then_inc(pads_made, 1)

        @block.scalar
        def _(act):
            def keep_qkg(n, th, outside):
                for kind in range(KINDS):
                    act.wait_ge(projected, KINDS * (SIDE * n + th) + kind + 1)
                    to = QKG[:, kind, :, 0:TOKCOLS, th]
                    if outside:
                        nc.scalar.activation(to, zeros[:, :].rearrange("p (r t) -> p r t", r=PATCH),
                                             ACT.Copy).then_inc(qkg_kept, 1)
                    else:
                        nc.scalar.activation(to, PS[:, kind, 0:WIDTH].rearrange("p (t r) -> p r t", r=PATCH),
                                             ACT.Identity, bias=bias[:, kind:kind + 1]).then_inc(qkg_kept, 1)

            def keep_strip(n, slot, tail):
                for th in range(SIDE - 1):
                    keep_qkg(n, th, False)
                if slot == SLOTS - 1 and not isinstance(tail, bool):
                    with act.If(tail):
                        keep_qkg(n, SIDE - 1, True)
                    with act.Else():
                        keep_qkg(n, SIDE - 1, False)
                else:
                    keep_qkg(n, SIDE - 1, tail)

            def strip(i, slot, last):
                n = i * SLOTS + slot
                for g in range(GROUPS):
                    act.wait_ge(maxed, GROUPS * n + g + 1)
                    nc.scalar.activation(E[:, g, :], S[:, g, :], ACT.Exp, bias=negmax[:, g:g + 1],
                                         accum_out=rowsum[:, g:g + 1]).then_inc(exped, 1)
                for g in range(GROUPS):
                    act.wait_ge(g_turned, GROUPS * n + g + 1)
                    b = WIDE_BANK[g]
                    nc.scalar.activation(GT[:, g, :, :].rearrange("p r c -> p (r c)"),
                                         PS[:, b:b + 2, :].rearrange("p b c -> p (b c)"),
                                         ACT.Copy).then_inc(g_kept, 1)
                for g in range(GROUPS):
                    act.wait_ge(mixed, GROUPS * n + g + 1)
                    b = WIDE_BANK[g]
                    for h in range(2):
                        lanes = slice(64 * h, 64 * h + 64)
                        nc.scalar.activation(o_place(lanes, h, g), o_bank(lanes, b), ACT.Copy).then_inc(o_high, 1)
                if slot < SLOTS - 1:
                    if last:
                        keep_strip(n + 1, slot + 1, slot + 1 == SLOTS - 1)
                    elif slot + 1 == SLOTS - 1:
                        keep_strip(n + 1, slot + 1, i % PER_IMAGE == PER_IMAGE - 1)
                    else:
                        keep_strip(n + 1, slot + 1, False)
                elif not last:
                    keep_strip(n + 1, 0, False)

            act.wait_ge(w_ready, 1)
            act.wait_ge(pads_made, 2 + 1 + KINDS)
            keep_strip(0, 0, False)
            with act.Fori(0, PASSES - 1) as i:
                for slot in range(SLOTS):
                    strip(i, slot, False)
            for slot in range(SLOTS):
                strip(PASSES - 1, slot, True)

        @block.vector
        def _(dve):
            dve.wait_ge(small_loaded, 16 * (2 + ROWS * HALVES + HALVES))
            dve.wait_ge(pads_made, 2)
            for a in range(HALVES):
                nc.vector.tensor_copy(w_st[:, a, :, a], w_nat[:, :]).then_inc(w_stretched, 1)
                for m in range(2):
                    for h in range(2):
                        nc.vector.tensor_copy(wo_st[:, m, a, h, m, a, :], wo_nat[:, :]).then_inc(w_stretched, 1)
            dve.wait_ge(w_turned, 1)
            nc.vector.tensor_copy(W[:, :, :].rearrange("p k (a o) -> p a k o", a=HALVES),
                                  PS[:, 0, 0:HALVES * KINDS * C1].rearrange("p (a k o) -> p a k o", a=HALVES, k=KINDS))
            nc.vector.tensor_copy(bias[:, :], PS[:, 2, 0:KINDS + 1])
            nc.vector.tensor_scalar(mask[:, :], PS[:, 2, 128:256], 1.0, BIG, ALU.subtract, ALU.mult)
            wo_ps = PS[:, 1, 0:2 * HALVES * CH].rearrange("p (m a c) -> p m a c", m=2, a=HALVES)
            nc.vector.tensor_copy(WOH[:, :, :, :].rearrange("p m c a -> p m a c"), wo_ps).then_inc(w_high, 1)
            dve.wait_ge(w_high, 1)
            nc.vector.tensor_tensor(WOL[:, :, :, :].rearrange("p m c a -> p m a c"), wo_ps,
                                    WOH[:, :, :, :].bitcast(fp32).rearrange("p m c a -> p m a c"),
                                    ALU.subtract).then_inc(w_ready, 1)

            def strip(i, slot):
                n = i * SLOTS + slot
                for g in range(GROUPS):
                    dve.wait_ge(scored, GROUPS * n + g + 1)
                    nc.vector.tensor_tensor(S[:, g, :], PS[:, SCORE_BANK[g], 0:TOK], mask[:, :],
                                            ALU.add).then_inc(masked, 1)
                    dve.wait_ge(masked, GROUPS * n + g + 1)
                    nc.vector.tensor_reduce(negmax[:, g:g + 1], S[:, g, :], AX.X, ALU.max,
                                            negate=True).then_inc(maxed, 1)
                for g in range(GROUPS):
                    dve.wait_ge(exped, GROUPS * n + g + 1)
                    nc.vector.reciprocal(inverse[:, g:g + 1], rowsum[:, g:g + 1]).then_inc(inverted, 1)
                    dve.wait_ge(inverted, GROUPS * n + g + 1)
                    nc.vector.tensor_scalar(P[:, g, :], E[:, g, :], inverse[:, g:g + 1], None,
                                            ALU.mult).then_inc(normed, 1)
                for g in range(GROUPS):
                    dve.wait_ge(p_turned, GROUPS * n + g + 1)
                    nc.vector.tensor_copy(PT[:, g, :], PS[:, PT_BANK[g], 0:TOK]).then_inc(p_kept, 1)
                for g in range(GROUPS):
                    b = WIDE_BANK[g]
                    for h in range(2):
                        dve.wait_ge(o_high, 2 * (GROUPS * n + g) + h + 1)
                        lanes = slice(64 * h, 64 * h + 64)
                        low = slice(64 - 64 * h, 128 - 64 * h)
                        nc.vector.tensor_tensor(o_place(low, h, g), o_bank(lanes, b),
                                                o_place(lanes, h, g).bitcast(fp32),
                                                ALU.subtract).then_inc(o_low, 1)
                for th in range(SIDE):
                    for pair in range(2):
                        dve.wait_ge(out_made, 2 * (SIDE * n + th) + pair + 1)
                        b = OUT_BANK + 2 * pair
                        rows = X[:, slot, th, 2 * pair:2 * pair + 2, :]
                        nc.vector.scalar_tensor_tensor(
                            out=rows, in0=PS[:, b:b + 2, 0:WIDTH], scalar=bias[:, KINDS:KINDS + 1], in1=rows,
                            op0=ALU.add, op1=ALU.add).then_inc(out_kept, 1)

            with dve.Fori(0, PASSES - 1) as i:
                for slot in range(SLOTS):
                    strip(i, slot)
            for slot in range(SLOTS):
                strip(PASSES - 1, slot)

        @block.tensor
        def _(pe):
            pe.wait_ge(consts_made, 2)
            pe.wait_ge(w_stretched, 10)
            for a in range(HALVES):
                nc.tensor.transpose(PS[:, 0, a * KINDS * C1:(a + 1) * KINDS * C1],
                                    w_st[:, a, :, :].rearrange("k c a -> k (c a)"),
                                    ident[0:KINDS * C1, 0:KINDS * C1])
            for m in range(2):
                for a in range(HALVES):
                    j = m * HALVES + a
                    nc.tensor.transpose(PS[:, 1, j * CH:(j + 1) * CH],
                                        wo_st[:, m, a, :, :, :, :].rearrange("c h m a o -> c (h m a o)"),
                                        ident[0:CH, 0:CH])
            nc.tensor.transpose(PS[:, 2, 0:KINDS + 1], b_st[:, :], ident[0:KINDS + 1, 0:KINDS + 1])
            pattern = blocks8[:, :, :].rearrange("b k t -> b (k t)")
            nc.tensor.matmul(PS[:, 2, 128:256], pattern, pattern, start=True, stop=True).then_inc(w_turned, 1)
            pe.wait_ge(w_ready, 1)

            def project(i, n, slot, th):
                pe.wait_ge(x_loaded[slot][th], 16 * (i + 1))
                for kind in range(KINDS):
                    if th:
                        pe.wait_ge(qkg_kept, KINDS * (SIDE * n + th - 1) + kind + 1)
                    for r in range(ROWS):
                        lanes = slice(32 * r, 32 * r + 32)
                        mm = nc.tensor.matmul(PS[lanes, kind, 0:WIDTH], W[:, kind, :], X[:, slot, th, r, :],
                                              start=True, stop=True)
                    mm.then_inc(projected, 1)

            def attend(n):
                pe.wait_ge(qkg_kept, KINDS * SIDE * (n + 1))
                for g in range(GROUPS):
                    for col in range(PATCH):
                        mm = nc.tensor.matmul(PS[:, SCORE_BANK[g], 0:TOK], tokens(Q, col, g), tokens(K, col, g),
                                              start=(col == 0), stop=(col == PATCH - 1))
                    mm.then_inc(scored, 1)
                for g in range(GROUPS):
                    if g:
                        pe.wait_ge(masked, GROUPS * n + 1)
                    for col in range(PATCH):
                        c = col % 4
                        mm = nc.tensor.transpose(PS[:, WIDE_BANK[g] + col // 4, c * 128:(c + 1) * 128],
                                                 tokens(G, col, g), ident[:, :])
                    mm.then_inc(g_turned, 1)

                def turn_p(g):
                    pe.wait_ge(normed, GROUPS * n + g + 1)
                    nc.tensor.transpose(PS[:, PT_BANK[g], 0:TOK], P[:, g, :], ident[:, :]).then_inc(p_turned, 1)

                def mix(g, cols):
                    for col in cols:
                        c = col % 4
                        mm = nc.tensor.matmul(PS[:, WIDE_BANK[g] + col // 4, c * TOK:(c + 1) * TOK],
                                              GT[:, g, col, :], PT[:, g, :], start=True, stop=True)
                    return mm

                turn_p(0)
                pe.wait_ge(g_kept, GROUPS * n + 1)
                pe.wait_ge(p_kept, GROUPS * n + 1)
                mix(0, range(0, 4))
                turn_p(1)
                mix(0, range(4, 8)).then_inc(mixed, 1)
                pe.wait_ge(g_kept, GROUPS * n + 2)
                pe.wait_ge(p_kept, GROUPS * n + 2)
                mix(1, range(0, 8)).then_inc(mixed, 1)

            def project_out(n, th):
                if th == 0:
                    pe.wait_ge(o_high, 2 * GROUPS * (n + 1))
                    pe.wait_ge(o_low, 2 * GROUPS * (n + 1))
                for pair in range(2):
                    if th:
                        pe.wait_ge(out_kept, 2 * (SIDE * n + th - 1) + pair + 1)
                    for m in range(2):
                        for w in (WOH, WOL):
                            mm = nc.tensor.matmul(PS[:, OUT_BANK + 2 * pair + m, 0:WIDTH],
                                                  w[:, m, :, :].rearrange("p c a -> p (c a)"),
                                                  O[:, pair, th, 0:WIDTH], start=(w is WOH), stop=(w is WOL))
                    mm.then_inc(out_made, 1)

            def strip(i, slot, last):
                n = i * SLOTS + slot
                attend(n)
                for th in range(SIDE):
                    if not (last and slot == SLOTS - 1):
                        if th == 0:
                            pe.wait_ge(o_high, 2 * GROUPS * n + 2)
                            pe.wait_ge(o_low, 2 * GROUPS * n + 2)
                        project(i + (slot + 1) // SLOTS, n + 1, (slot + 1) % SLOTS, th)
                    project_out(n, th)

            for th in range(SIDE):
                project(0, 0, 0, th)
            with pe.Fori(0, PASSES - 1) as i:
                for slot in range(SLOTS):
                    strip(i, slot, False)
            for slot in range(SLOTS):
                strip(PASSES - 1, slot, True)


_INS = ["x", "L0_conv_w_ptg", "L0_conv_b_ptg", "L0_conv_w_out", "L0_conv_b_out"]


def kernel(**inputs):
    import numpy as _np
    import concourse.bacc as _bacc
    from concourse import mybir as _mybir
    from concourse.bass_utils import run_bass_kernel_spmd as _run

    nc = _bacc.Bacc("TRN2", target_bir_lowering=False, num_devices=1)
    arrays, args = {}, []
    for name in _INS:
        a = _np.ascontiguousarray(inputs[name])
        arrays[f"in_{name}_dram"] = a
        args.append(nc.dram_tensor(f"in_{name}_dram", a.shape, _mybir.dt.from_np(a.dtype), kind="ExternalInput").ap())
    shape = tuple(inputs["x"].shape)
    args.append(nc.dram_tensor("out_0_dram", shape, _mybir.dt.float32, kind="ExternalOutput").ap())
    block_attention_kernel(nc, *args)
    r = _run(nc, [arrays], core_ids=[0])
    return r.results[0]["out_0_dram"]
```

```python
import concourse.bass as bass
from concourse import mybir
from contextlib import ExitStack


def block_attention_kernel(nc, x, w_ptg, b_ptg, w_out, b_out, out):
    fp32 = mybir.dt.float32
    fp32r = mybir.dt.float32r
    ALU = mybir.AluOpType
    ACT = mybir.ActivationFunctionType
    AX = mybir.AxisListType

    IMAGES, CH, HEIGHT, WIDTH = x.shape
    C1 = w_out.shape[1]
    PATCH, SIDE = 8, 4
    STRIP = PATCH * SIDE
    HALVES = 2
    ROWS = PATCH // HALVES
    STRIPS = -(-HEIGHT // STRIP)
    SLOTS = 4
    PASSES = IMAGES * STRIPS // SLOTS
    PER_IMAGE = STRIPS // SLOTS
    TOKCOLS = WIDTH // PATCH
    PADCOLS = STRIPS * SIDE
    GROUPS = 2
    GCOLS = PADCOLS // GROUPS
    TOK = SIDE * GCOLS
    NEAR = TOK // 2
    KINDS = 3
    RUN = ROWS * WIDTH
    BIG = 1.0e37
    Q, K, G = range(KINDS)
    assert HALVES * CH == 128 and ROWS * HALVES * C1 == 128 and TOK == 128
    assert STRIPS % SLOTS == 0 and WIDTH <= 512

    x_d = x.rearrange("n c h w -> n c (h w)")
    out_d = out.rearrange("n c h w -> n c (h w)")

    ctx = ExitStack()
    with ctx:
        def sb(name, shape, dt=fp32):
            return ctx.enter_context(nc.sbuf_tensor(name, shape, dt))

        def sem(name):
            return ctx.enter_context(nc.semaphore(name))

        X = sb("X", [128, SLOTS, SIDE, ROWS, WIDTH])
        QKG = sb("QKG", [128, KINDS, PATCH, PADCOLS, SIDE])
        GT = sb("GT", [128, GROUPS, PATCH, 128])
        O = sb("O", [128, 2, SIDE, PADCOLS * PATCH], fp32r)
        S = sb("S", [128, GROUPS, NEAR])
        E = sb("E", [128, GROUPS, NEAR])
        P = sb("P", [128, GROUPS, TOK])
        PT = sb("PT", [128, GROUPS, TOK])
        negmax = sb("negmax", [128, GROUPS])
        rowsum = sb("rowsum", [128, GROUPS])
        inverse = sb("inverse", [128, GROUPS])
        zeros = sb("zeros", [128, PATCH * TOKCOLS])
        ident = sb("ident", [128, 128])
        blocks4 = sb("blocks4", [4, 2, 4, SIDE * SIDE])
        mask = sb("mask", [128, NEAR])
        w_nat = sb("w_nat", [KINDS * C1, CH])
        wo_nat = sb("wo_nat", [CH, C1])
        w_st = sb("w_st", [KINDS * C1, HALVES, CH, HALVES])
        wo_st = sb("wo_st", [CH, 2, HALVES, 2, 2, HALVES, C1])
        b_st = sb("b_st", [KINDS + 1, 128])
        W = sb("W", [128, KINDS, HALVES * C1])
        WOH = sb("WOH", [128, 2, CH, HALVES], fp32r)
        WOL = sb("WOL", [128, 2, CH, HALVES], fp32r)
        bias = sb("bias", [128, KINDS + 1])

        PS = ctx.enter_context(nc.psum_tensor("PS", [128, 8, 512], fp32))
        PROJ_BANK = (0, 3, 6, 7, 0, 3, 1, 2, 0, 3, 1, 2)
        SCORE_BANK = (3, 0)
        WIDE_BANK = (1, 4)
        PT_BANK = (6, 7)
        OUT_BANK = 4

        x_loaded = [[sem(f"x_loaded_{s}_{t}") for t in range(SIDE)] for s in range(SLOTS)]
        out_stored = [[sem(f"out_stored_{s}_{t}") for t in range(SIDE)] for s in range(SLOTS)]
        small_loaded = sem("small_loaded")
        ident_cleared = sem("ident_cleared")
        pads_made = sem("pads_made")
        consts_made = sem("consts_made")
        w_stretched = sem("w_stretched")
        w_turned = sem("w_turned")
        w_high = sem("w_high")
        w_ready = sem("w_ready")
        projected = sem("projected")
        qkg_kept = sem("qkg_kept")
        scored = sem("scored")
        masked = sem("masked")
        maxed = sem("maxed")
        exped = sem("exped")
        inverted = sem("inverted")
        normed = sem("normed")
        p_turned = sem("p_turned")
        p_kept = sem("p_kept")
        g_turned = sem("g_turned")
        g0_kept = sem("g0_kept")
        g1_kept = sem("g1_kept")
        mixed = sem("mixed")
        o_high = sem("o_high")
        o_low = sem("o_low")
        out_made = sem("out_made")
        out_kept = sem("out_kept")

        block = ctx.enter_context(nc.Block())

        def dram_rows(t, n, th, may_lack=False):
            row = n % STRIPS
            if may_lack:
                row = row % (STRIPS - 1)
            first = (row * STRIP + th * PATCH) * WIDTH
            return t[n // STRIPS, :, bass.ds(first, HALVES * RUN)]

        def slot_rows(slot, th):
            return X[:, slot, th, :, :].rearrange("p r w -> p (r w)")

        def tokens(kind, col, g):
            return QKG[:, kind, col, g * GCOLS:(g + 1) * GCOLS, :].rearrange("p t s -> p (t s)")

        def o_bank(lanes, b):
            return PS[lanes, b:b + 2, :].rearrange("p b (r t s) -> p (b r) t s", r=PATCH // 2, s=SIDE)

        def o_place(lanes, h, g):
            whole = O[lanes, h, :, :].rearrange("p s (t r) -> p r t s", r=PATCH)
            return whole[:, :, g * GCOLS:(g + 1) * GCOLS, :]

        @block.sync
        def _(sp):
            sp.dma_start(w_nat[:, :], w_ptg).then_inc(small_loaded, 16)
            sp.dma_start(wo_nat[:, :], w_out).then_inc(small_loaded, 16)
            for j in range(ROWS * HALVES):
                sp.dma_start(b_st[0:KINDS, j * C1:(j + 1) * C1],
                             b_ptg.rearrange("(k o) -> k o", k=KINDS)).then_inc(small_loaded, 16)
            with nc.allow_non_contiguous_dma(reason="64 values, once"):
                for a in range(HALVES):
                    sp.dma_start(b_st[KINDS:KINDS + 1, a:128:HALVES],
                                 b_out.rearrange("(k c) -> k c", k=1)).then_inc(small_loaded, 16)

            def load(n, slot, th):
                if slot == SLOTS - 1 and th == SIDE - 1:
                    sp.dma_start(slot_rows(slot, th), dram_rows(x_d, n, th, True),
                                 cond=(n % STRIPS < STRIPS - 1)).then_inc(x_loaded[slot][th], 16)
                else:
                    sp.dma_start(slot_rows(slot, th), dram_rows(x_d, n, th)).then_inc(x_loaded[slot][th], 16)

            def store(n, slot, th):
                if slot == SLOTS - 1 and th == SIDE - 1:
                    sp.dma_start(dram_rows(out_d, n, th, True), slot_rows(slot, th),
                                 cond=(n % STRIPS < STRIPS - 1)).then_inc(out_stored[slot][th], 16)
                else:
                    sp.dma_start(dram_rows(out_d, n, th), slot_rows(slot, th)).then_inc(out_stored[slot][th], 16)

            def strip(i, slot, last):
                n = i * SLOTS + slot
                ahead = (slot + SLOTS - 1) % SLOTS
                for th in range(SIDE):
                    if not last or slot == 0:
                        sp.wait_ge(out_stored[ahead][th], 16 * (i + (2 if slot else 1)))
                        load(n + SLOTS - 1, ahead, th)
                    sp.wait_ge(out_kept, 2 * (SIDE * n + th + 1))
                    if not (last and slot == SLOTS - 1 and th == SIDE - 1):
                        store(n, slot, th)

            for slot in range(SLOTS - 1):
                for th in range(SIDE):
                    load(slot, slot, th)
            for slot in range(SLOTS):
                for th in range(SIDE):
                    sp.sem_inc(out_stored[slot][th], 16)
            with sp.Fori(0, PASSES - 1) as i:
                for slot in range(SLOTS):
                    strip(i, slot, False)
            for slot in range(SLOTS):
                strip(PASSES - 1, slot, True)
            for slot in range(SLOTS):
                for th in range(SIDE):
                    stores = 1 + PASSES - (slot == SLOTS - 1 and th == SIDE - 1)
                    sp.wait_ge(out_stored[slot][th], 16 * stores)

        @block.gpsimd
        def _(pool):
            nc.gpsimd.memset(ident[:, :], 0.0).then_inc(ident_cleared, 1)
            nc.gpsimd.memset(blocks4[:, :, :, :], 0.0).then_inc(ident_cleared, 1)
            nc.gpsimd.memset(w_st[:, :, :, :], 0.0).then_inc(pads_made, 1)
            nc.gpsimd.memset(wo_st[:, :, :, :, :, :, :], 0.0).then_inc(pads_made, 1)
            pool.wait_ge(ident_cleared, 2)
            nc.gpsimd.affine_select(out=ident[:, :], in_=ident[:, :], compare_op=ALU.not_equal, fill=1.0,
                                    base=0, pattern=[[-1, 128]], channel_multiplier=1).then_inc(consts_made, 1)
            nc.gpsimd.affine_select(out=blocks4[:, :, :, :], in_=blocks4[:, :, :, :],
                                    compare_op=ALU.not_equal, fill=1.0, base=0,
                                    pattern=[[0, 2], [-1, 4], [0, SIDE * SIDE]],
                                    channel_multiplier=1).then_inc(consts_made, 1)
            nc.gpsimd.memset(zeros[:, :], 0.0).then_inc(pads_made, 1)
            nc.gpsimd.memset(P[:, :, :], 0.0).then_inc(pads_made, 1)
            for kind in range(KINDS):
                nc.gpsimd.memset(QKG[:, kind, :, TOKCOLS:PADCOLS, :], 0.0).then_inc(pads_made, 1)

        @block.scalar
        def _(act):
            def keep(n, th, kind, outside):
                act.wait_ge(projected, KINDS * (SIDE * n + th) + kind + 1)
                to = QKG[:, kind, :, 0:TOKCOLS, th]
                if outside:
                    nc.scalar.activation(to, zeros[:, :].rearrange("p (r t) -> p r t", r=PATCH),
                                         ACT.Copy).then_inc(qkg_kept, 1)
                else:
                    bank = PROJ_BANK[KINDS * th + kind]
                    nc.scalar.activation(to, PS[:, bank, 0:WIDTH].rearrange("p (t r) -> p r t", r=PATCH),
                                         ACT.Identity, bias=bias[:, kind:kind + 1]).then_inc(qkg_kept, 1)

            def keep_rest(n, at_end):
                for th in range(SIDE - 1):
                    for kind in range(KINDS):
                        if th or kind:
                            keep(n, th, kind, False)
                if isinstance(at_end, bool):
                    for kind in range(KINDS):
                        keep(n, SIDE - 1, kind, at_end)
                else:
                    with act.If(at_end):
                        for kind in range(KINDS):
                            keep(n, SIDE - 1, kind, True)
                    with act.Else():
                        for kind in range(KINDS):
                            keep(n, SIDE - 1, kind, False)

            def keep_pt(n, g):
                act.wait_ge(p_turned, GROUPS * n + g + 1)
                nc.scalar.activation(PT[:, g, :], PS[:, PT_BANK[g], 0:TOK], ACT.Copy).then_inc(p_kept, 1)

            def strip(i, slot, last):
                n = i * SLOTS + slot
                more = not (last and slot == SLOTS - 1)
                for g in range(GROUPS):
                    act.wait_ge(maxed, GROUPS * n + g + 1)
                    nc.scalar.activation(E[:, g, :], S[:, g, :], ACT.Exp, bias=negmax[:, g:g + 1],
                                         accum_out=rowsum[:, g:g + 1]).then_inc(exped, 1)
                act.wait_ge(g_turned, GROUPS * n + 1)
                nc.scalar.activation(GT[:, 0, :, :].rearrange("p r c -> p (r c)"),
                                     PS[:, WIDE_BANK[0]:WIDE_BANK[0] + 2, :].rearrange("p b c -> p (b c)"),
                                     ACT.Copy).then_inc(g0_kept, 1)
                keep_pt(n, 0)
                if more:
                    keep(n + 1, 0, Q, False)
                keep_pt(n, 1)
                for g in range(GROUPS):
                    act.wait_ge(mixed, GROUPS * n + g + 1)
                    b = WIDE_BANK[g]
                    for h in range(2):
                        lanes = slice(64 * h, 64 * h + 64)
                        nc.scalar.activation(o_place(lanes, h, g), o_bank(lanes, b), ACT.Copy).then_inc(o_high, 1)
                if more:
                    at_end = slot + 1 == SLOTS - 1
                    if at_end and not last:
                        at_end = i % PER_IMAGE == PER_IMAGE - 1
                    keep_rest(n + 1, at_end)

            act.wait_ge(w_ready, 1)
            act.wait_ge(pads_made, 2 + 2 + KINDS)
            keep(0, 0, Q, False)
            keep_rest(0, False)
            with act.Fori(0, PASSES - 1) as i:
                for slot in range(SLOTS):
                    strip(i, slot, False)
            for slot in range(SLOTS):
                strip(PASSES - 1, slot, True)

        @block.vector
        def _(dve):
            dve.wait_ge(small_loaded, 16 * (2 + ROWS * HALVES + HALVES))
            dve.wait_ge(pads_made, 2)
            for a in range(HALVES):
                nc.vector.tensor_copy(w_st[:, a, :, a], w_nat[:, :]).then_inc(w_stretched, 1)
                for m in range(2):
                    for h in range(2):
                        nc.vector.tensor_copy(wo_st[:, m, a, h, m, a, :], wo_nat[:, :]).then_inc(w_stretched, 1)
            dve.wait_ge(w_turned, 1)
            nc.vector.tensor_copy(W[:, :, :].rearrange("p k (a o) -> p a k o", a=HALVES),
                                  PS[:, 0, 0:HALVES * KINDS * C1].rearrange("p (a k o) -> p a k o", a=HALVES, k=KINDS))
            nc.vector.tensor_copy(bias[:, :], PS[:, 2, 0:KINDS + 1])
            nc.vector.tensor_scalar(mask[:, :], PS[:, 2, 128:128 + NEAR], 1.0, BIG, ALU.subtract, ALU.mult)
            wo_ps = PS[:, 1, 0:2 * HALVES * CH].rearrange("p (m a c) -> p m a c", m=2, a=HALVES)
            nc.vector.tensor_copy(WOH[:, :, :, :].rearrange("p m c a -> p m a c"), wo_ps).then_inc(w_high, 1)
            dve.wait_ge(w_high, 1)
            nc.vector.tensor_tensor(WOL[:, :, :, :].rearrange("p m c a -> p m a c"), wo_ps,
                                    WOH[:, :, :, :].bitcast(fp32).rearrange("p m c a -> p m a c"),
                                    ALU.subtract).then_inc(w_ready, 1)

            def strip(i, slot):
                n = i * SLOTS + slot
                for g in range(GROUPS):
                    dve.wait_ge(scored, GROUPS * n + g + 1)
                    nc.vector.tensor_tensor(S[:, g, :], PS[:, SCORE_BANK[g], 0:NEAR], mask[:, :],
                                            ALU.add).then_inc(masked, 1)
                    dve.wait_ge(masked, GROUPS * n + g + 1)
                    nc.vector.tensor_reduce(negmax[:, g:g + 1], S[:, g, :], AX.X, ALU.max,
                                            negate=True).then_inc(maxed, 1)
                for g in range(GROUPS):
                    dve.wait_ge(exped, GROUPS * n + g + 1)
                    nc.vector.reciprocal(inverse[:, g:g + 1], rowsum[:, g:g + 1]).then_inc(inverted, 1)
                    dve.wait_ge(inverted, GROUPS * n + g + 1)
                    for h in range(2):
                        half = slice(NEAR * h, NEAR * (h + 1))
                        nc.vector.tensor_scalar(P[half, g, half], E[half, g, :], inverse[half, g:g + 1], None,
                                                ALU.mult).then_inc(normed, 1)
                dve.wait_ge(g_turned, GROUPS * n + 2)
                nc.vector.tensor_copy(GT[:, 1, :, :].rearrange("p r c -> p (r c)"),
                                      PS[:, WIDE_BANK[1]:WIDE_BANK[1] + 2, :].rearrange("p b c -> p (b c)")
                                      ).then_inc(g1_kept, 1)
                for g in range(GROUPS):
                    b = WIDE_BANK[g]
                    for h in range(2):
                        dve.wait_ge(o_high, 2 * (GROUPS * n + g) + h + 1)
                        lanes = slice(64 * h, 64 * h + 64)
                        low = slice(64 - 64 * h, 128 - 64 * h)
                        nc.vector.tensor_tensor(o_place(low, h, g), o_bank(lanes, b),
                                                o_place(lanes, h, g).bitcast(fp32),
                                                ALU.subtract).then_inc(o_low, 1)
                for th in range(SIDE):
                    for pair in range(2):
                        dve.wait_ge(out_made, 2 * (SIDE * n + th) + pair + 1)
                        b = OUT_BANK + 2 * pair
                        rows = X[:, slot, th, 2 * pair:2 * pair + 2, :]
                        nc.vector.scalar_tensor_tensor(
                            out=rows, in0=PS[:, b:b + 2, 0:WIDTH], scalar=bias[:, KINDS:KINDS + 1], in1=rows,
                            op0=ALU.add, op1=ALU.add).then_inc(out_kept, 1)

            dve.wait_ge(pads_made, 2 + 2 + KINDS)
            with dve.Fori(0, PASSES - 1) as i:
                for slot in range(SLOTS):
                    strip(i, slot)
            for slot in range(SLOTS):
                strip(PASSES - 1, slot)

        @block.tensor
        def _(pe):
            pe.wait_ge(consts_made, 2)
            pe.wait_ge(w_stretched, 10)
            for a in range(HALVES):
                nc.tensor.transpose(PS[:, 0, a * KINDS * C1:(a + 1) * KINDS * C1],
                                    w_st[:, a, :, :].rearrange("k c a -> k (c a)"),
                                    ident[0:KINDS * C1, 0:KINDS * C1])
            for m in range(2):
                for a in range(HALVES):
                    j = m * HALVES + a
                    nc.tensor.transpose(PS[:, 1, j * CH:(j + 1) * CH],
                                        wo_st[:, m, a, :, :, :, :].rearrange("c h m a o -> c (h m a o)"),
                                        ident[0:CH, 0:CH])
            nc.tensor.transpose(PS[:, 2, 0:KINDS + 1], b_st[:, :], ident[0:KINDS + 1, 0:KINDS + 1])
            pattern = blocks4[:, :, :, :].rearrange("b h k t -> b (h k t)")
            nc.tensor.matmul(PS[:, 2, 128:128 + NEAR], pattern, pattern[:, 0:NEAR], start=True, stop=True).then_inc(w_turned, 1)
            pe.wait_ge(w_ready, 1)

            def project(i, n, slot, th, kinds):
                for kind in kinds:
                    j = KINDS * th + kind
                    if kind == Q:
                        pe.wait_ge(x_loaded[slot][th], 16 * (i + 1))
                    if j >= 4 and j not in (6, 7):
                        pe.wait_ge(qkg_kept, KINDS * SIDE * n + j - 3)
                    for r in range(ROWS):
                        lanes = slice(32 * r, 32 * r + 32)
                        mm = nc.tensor.matmul(PS[lanes, PROJ_BANK[j], 0:WIDTH], W[:, kind, :],
                                              X[:, slot, th, r, :], start=True, stop=True)
                    mm.then_inc(projected, 1)

            def score(n, g):
                for col in range(PATCH):
                    for h in range(2):
                        half = slice(NEAR * h, NEAR * (h + 1))
                        mm = nc.tensor.matmul(PS[half, SCORE_BANK[g], 0:NEAR], tokens(Q, col, g)[:, half],
                                              tokens(K, col, g)[:, half],
                                              start=(col == 0), stop=(col == PATCH - 1))
                mm.then_inc(scored, 1)

            def turn_g(n, g):
                for col in range(PATCH):
                    c = col % 4
                    mm = nc.tensor.transpose(PS[:, WIDE_BANK[g] + col // 4, c * 128:(c + 1) * 128],
                                             tokens(G, col, g), ident[:, :])
                mm.then_inc(g_turned, 1)

            def turn_p(n, g):
                pe.wait_ge(normed, 2 * (GROUPS * n + g + 1))
                nc.tensor.transpose(PS[:, PT_BANK[g], 0:TOK], P[:, g, :], ident[:, :]).then_inc(p_turned, 1)

            def mix(g, cols):
                for col in cols:
                    c = col % 4
                    mm = nc.tensor.matmul(PS[:, WIDE_BANK[g] + col // 4, c * TOK:(c + 1) * TOK],
                                          GT[:, g, col, :], PT[:, g, :], start=True, stop=True)
                return mm

            def project_out(n, th, more):
                for pair in range(2):
                    if th:
                        pe.wait_ge(out_kept, 2 * (SIDE * n + th - 1) + pair + 1)
                    elif pair and more:
                        pe.wait_ge(qkg_kept, KINDS * SIDE * (n + 1) + 4)
                    for m in range(2):
                        for w in (WOH, WOL):
                            mm = nc.tensor.matmul(PS[:, OUT_BANK + 2 * pair + m, 0:WIDTH],
                                                  w[:, m, :, :].rearrange("p c a -> p (c a)"),
                                                  O[:, pair, th, 0:WIDTH], start=(w is WOH), stop=(w is WOL))
                    mm.then_inc(out_made, 1)

            def strip(i, slot, last):
                n = i * SLOTS + slot
                more = not (last and slot == SLOTS - 1)
                ahead = (i + (slot + 1) // SLOTS, n + 1, (slot + 1) % SLOTS)
                pe.wait_ge(qkg_kept, KINDS * SIDE * (n + 1))
                score(n, 0)
                score(n, 1)
                turn_g(n, 0)
                pe.wait_ge(masked, GROUPS * n + 1)
                turn_g(n, 1)
                turn_p(n, 0)
                if more:
                    pe.wait_ge(masked, GROUPS * n + 2)
                    project(*ahead, 0, (Q,))
                pe.wait_ge(g0_kept, n + 1)
                pe.wait_ge(p_kept, GROUPS * n + 1)
                mix(0, range(0, 4))
                turn_p(n, 1)
                mix(0, range(4, 8)).then_inc(mixed, 1)
                pe.wait_ge(g1_kept, n + 1)
                pe.wait_ge(p_kept, GROUPS * n + 2)
                mix(1, range(0, 8)).then_inc(mixed, 1)
                if more:
                    project(*ahead, 0, (K, G))
                    project(*ahead, 1, (Q, K, G))
                pe.wait_ge(o_high, 2 * GROUPS * (n + 1))
                pe.wait_ge(o_low, 2 * GROUPS * (n + 1))
                project_out(n, 0, more)
                if more:
                    project(*ahead, 2, (Q, K, G))
                project_out(n, 1, more)
                if more:
                    project(*ahead, 3, (Q, K, G))
                project_out(n, 2, more)
                project_out(n, 3, more)

            for th in range(SIDE):
                project(0, 0, 0, th, (Q, K, G))
            with pe.Fori(0, PASSES - 1) as i:
                for slot in range(SLOTS):
                    strip(i, slot, False)
            for slot in range(SLOTS):
                strip(PASSES - 1, slot, True)


_INS = ["x", "L0_conv_w_ptg", "L0_conv_b_ptg", "L0_conv_w_out", "L0_conv_b_out"]


def kernel(**inputs):
    import numpy as _np
    import concourse.bacc as _bacc
    from concourse import mybir as _mybir
    from concourse.bass_utils import run_bass_kernel_spmd as _run

    nc = _bacc.Bacc("TRN2", target_bir_lowering=False, num_devices=1)
    arrays, args = {}, []
    for name in _INS:
        a = _np.ascontiguousarray(inputs[name])
        arrays[f"in_{name}_dram"] = a
        args.append(nc.dram_tensor(f"in_{name}_dram", a.shape, _mybir.dt.from_np(a.dtype), kind="ExternalInput").ap())
    shape = tuple(inputs["x"].shape)
    args.append(nc.dram_tensor("out_0_dram", shape, _mybir.dt.float32, kind="ExternalOutput").ap())
    block_attention_kernel(nc, *args)
    r = _run(nc, [arrays], core_ids=[0])
    return r.results[0]["out_0_dram"]
```

```python
import concourse.bass as bass
from concourse import mybir
from contextlib import ExitStack


def block_attention_kernel(nc, x, w_ptg, b_ptg, w_out, b_out, out):
    fp32 = mybir.dt.float32
    fp32r = mybir.dt.float32r
    ALU = mybir.AluOpType
    ACT = mybir.ActivationFunctionType
    AX = mybir.AxisListType

    IMAGES, CH, HEIGHT, WIDTH = x.shape
    C1 = w_out.shape[1]
    PATCH, SIDE = 8, 4
    STRIP = PATCH * SIDE
    HALVES = 2
    ROWS = PATCH // HALVES
    STRIPS = -(-HEIGHT // STRIP)
    SLOTS = 4
    PASSES = IMAGES * STRIPS // SLOTS
    PER_IMAGE = STRIPS // SLOTS
    TOKCOLS = WIDTH // PATCH
    PADCOLS = STRIPS * SIDE
    GROUPS = 2
    GCOLS = PADCOLS // GROUPS
    TOK = SIDE * GCOLS
    NEAR = TOK // 2
    KINDS = 3
    RUN = ROWS * WIDTH
    BIG = 1.0e37
    Q, K, G = range(KINDS)
    assert HALVES * CH == 128 and ROWS * HALVES * C1 == 128 and TOK == 128
    assert STRIPS % SLOTS == 0 and WIDTH <= 512

    x_d = x.rearrange("n c h w -> n c (h w)")
    out_d = out.rearrange("n c h w -> n c (h w)")

    ctx = ExitStack()
    with ctx:
        def sb(name, shape, dt=fp32):
            return ctx.enter_context(nc.sbuf_tensor(name, shape, dt))

        def sem(name):
            return ctx.enter_context(nc.semaphore(name))

        X = sb("X", [128, SLOTS, SIDE, ROWS, WIDTH])
        QKG = sb("QKG", [128, KINDS, PATCH, PADCOLS, SIDE])
        GT = sb("GT", [128, GROUPS, PATCH, 128])
        O = sb("O", [128, 2, SIDE, PADCOLS * PATCH], fp32r)
        S = sb("S", [128, GROUPS, NEAR])
        E = sb("E", [128, GROUPS, NEAR])
        P = sb("P", [128, GROUPS, TOK])
        PT = sb("PT", [128, GROUPS, TOK])
        negmax = sb("negmax", [128, GROUPS])
        rowsum = sb("rowsum", [128, GROUPS])
        inverse = sb("inverse", [128, GROUPS])
        zeros = sb("zeros", [128, PATCH * TOKCOLS])
        ident = sb("ident", [128, 128])
        blocks4 = sb("blocks4", [4, 2, 4, SIDE * SIDE])
        mask = sb("mask", [128, NEAR])
        w_nat = sb("w_nat", [KINDS * C1, CH])
        wo_nat = sb("wo_nat", [CH, C1])
        w_st = sb("w_st", [KINDS * C1, HALVES, CH, HALVES])
        wo_st = sb("wo_st", [CH, 2, HALVES, 2, 2, HALVES, C1])
        b_nat = sb("b_nat", [KINDS, C1])
        bo_nat = sb("bo_nat", [1, CH])
        b_st = sb("b_st", [KINDS, HALVES * ROWS, C1])
        bo_st = sb("bo_st", [1, CH, HALVES])
        W = sb("W", [128, KINDS, HALVES * C1])
        WOH = sb("WOH", [128, 2, CH, HALVES], fp32r)
        WOL = sb("WOL", [128, 2, CH, HALVES], fp32r)
        bias = sb("bias", [128, KINDS + 1])

        PS = ctx.enter_context(nc.psum_tensor("PS", [128, 8, 512], fp32))
        PROJ_BANK = (0, 3, 6, 7, 0, 3, 1, 2, 0, 3, 1, 2)
        SCORE_BANK = (3, 0)
        WIDE_BANK = (1, 4)
        PT_BANK = 3
        OUT_BANK = 4

        x_loaded = [[sem(f"x_loaded_{s}_{t}") for t in range(SIDE)] for s in range(SLOTS)]
        out_stored = [[sem(f"out_stored_{s}_{t}") for t in range(SIDE)] for s in range(SLOTS)]
        small_loaded = sem("small_loaded")
        ident_cleared = sem("ident_cleared")
        zeros_made = sem("zeros_made")
        pads_made = sem("pads_made")
        consts_made = sem("consts_made")
        w_stretched = sem("w_stretched")
        w_turned = sem("w_turned")
        w_ready = sem("w_ready")
        wo_high = sem("wo_high")
        wo_ready = sem("wo_ready")
        projected = sem("projected")
        qkg_kept = sem("qkg_kept")
        scored = sem("scored")
        masked = sem("masked")
        maxed = sem("maxed")
        exped = sem("exped")
        inverted = sem("inverted")
        normed = sem("normed")
        p_turned = sem("p_turned")
        p_kept = sem("p_kept")
        g_turned = sem("g_turned")
        g0_kept = sem("g0_kept")
        g1_kept = sem("g1_kept")
        mixed = sem("mixed")
        o_high = sem("o_high")
        o_low = sem("o_low")
        out_made = sem("out_made")
        out_kept = sem("out_kept")

        block = ctx.enter_context(nc.Block())

        def dram_rows(t, n, th, may_lack=False):
            row = n % STRIPS
            if may_lack:
                row = row % (STRIPS - 1)
            first = (row * STRIP + th * PATCH) * WIDTH
            return t[n // STRIPS, :, bass.ds(first, HALVES * RUN)]

        def slot_rows(slot, th):
            return X[:, slot, th, :, :].rearrange("p r w -> p (r w)")

        def tokens(kind, col, g):
            return QKG[:, kind, col, g * GCOLS:(g + 1) * GCOLS, :].rearrange("p t s -> p (t s)")

        def o_bank(lanes, b):
            return PS[lanes, b:b + 2, :].rearrange("p b (r t s) -> p (b r) t s", r=PATCH // 2, s=SIDE)

        def o_place(lanes, h, g):
            whole = O[lanes, h, :, :].rearrange("p s (t r) -> p r t s", r=PATCH)
            return whole[:, :, g * GCOLS:(g + 1) * GCOLS, :]

        @block.sync
        def _(sp):
            sp.dma_start(w_nat[:, :], w_ptg).then_inc(small_loaded, 16)
            sp.dma_start(wo_nat[:, :], w_out).then_inc(small_loaded, 16)
            sp.dma_start(b_nat[:, :], b_ptg.rearrange("(k o) -> k o", k=KINDS)).then_inc(small_loaded, 16)
            sp.dma_start(bo_nat[:, :], b_out.rearrange("(k c) -> k c", k=1)).then_inc(small_loaded, 16)
            def load(n, slot, th):
                if slot == SLOTS - 1 and th == SIDE - 1:
                    sp.dma_start(slot_rows(slot, th), dram_rows(x_d, n, th, True),
                                 cond=(n % STRIPS < STRIPS - 1)).then_inc(x_loaded[slot][th], 16)
                else:
                    sp.dma_start(slot_rows(slot, th), dram_rows(x_d, n, th)).then_inc(x_loaded[slot][th], 16)

            def store(n, slot, th):
                if slot == SLOTS - 1 and th == SIDE - 1:
                    sp.dma_start(dram_rows(out_d, n, th, True), slot_rows(slot, th),
                                 cond=(n % STRIPS < STRIPS - 1)).then_inc(out_stored[slot][th], 16)
                else:
                    sp.dma_start(dram_rows(out_d, n, th), slot_rows(slot, th)).then_inc(out_stored[slot][th], 16)

            def strip(i, slot, last):
                n = i * SLOTS + slot
                ahead = (slot + SLOTS - 1) % SLOTS
                for th in range(SIDE):
                    if not last or slot == 0:
                        sp.wait_ge(out_stored[ahead][th], 16 * (i + (2 if slot else 1)))
                        load(n + SLOTS - 1, ahead, th)
                    if not (last and slot == SLOTS - 1 and th == SIDE - 1):
                        sp.wait_ge(out_kept, 2 * (SIDE * n + th + 1))
                        store(n, slot, th)

            for slot in range(SLOTS - 1):
                for th in range(SIDE):
                    load(slot, slot, th)
            for slot in range(SLOTS):
                for th in range(SIDE):
                    sp.sem_inc(out_stored[slot][th], 16)
            with sp.Fori(0, PASSES - 1) as i:
                for slot in range(SLOTS):
                    strip(i, slot, False)
            for slot in range(SLOTS):
                strip(PASSES - 1, slot, True)
            for slot in range(SLOTS):
                for th in range(SIDE):
                    stores = 1 + PASSES - (slot == SLOTS - 1 and th == SIDE - 1)
                    sp.wait_ge(out_stored[slot][th], 16 * stores)

        @block.gpsimd
        def _(pool):
            nc.gpsimd.memset(zeros[:, :], 0.0).then_inc(zeros_made, 1)
            nc.gpsimd.memset(ident[:, :], 0.0).then_inc(ident_cleared, 1)
            nc.gpsimd.memset(blocks4[:, :, :, :], 0.0).then_inc(ident_cleared, 1)
            nc.gpsimd.memset(w_st[:, :, :, :], 0.0).then_inc(pads_made, 1)
            nc.gpsimd.memset(wo_st[:, :, :, :, :, :, :], 0.0).then_inc(pads_made, 1)
            pool.wait_ge(ident_cleared, 2)
            nc.gpsimd.affine_select(out=ident[:, :], in_=ident[:, :], compare_op=ALU.not_equal, fill=1.0,
                                    base=0, pattern=[[-1, 128]], channel_multiplier=1).then_inc(consts_made, 1)
            nc.gpsimd.affine_select(out=blocks4[:, :, :, :], in_=blocks4[:, :, :, :],
                                    compare_op=ALU.not_equal, fill=1.0, base=0,
                                    pattern=[[0, 2], [-1, 4], [0, SIDE * SIDE]],
                                    channel_multiplier=1).then_inc(consts_made, 1)
            nc.gpsimd.memset(P[:, :, :], 0.0).then_inc(pads_made, 1)
            for kind in range(KINDS):
                nc.gpsimd.memset(QKG[:, kind, :, TOKCOLS:PADCOLS, :], 0.0).then_inc(pads_made, 1)

        @block.scalar
        def _(act):
            act.wait_ge(zeros_made, 1)
            nc.scalar.activation(E[:, 0, 0:1], zeros[:, 0:1], ACT.Exp)

            def keep(n, th, kind, outside):
                act.wait_ge(projected, KINDS * (SIDE * n + th) + kind + 1)
                to = QKG[:, kind, :, 0:TOKCOLS, th]
                if outside:
                    nc.scalar.activation(to, zeros[:, :].rearrange("p (r t) -> p r t", r=PATCH),
                                         ACT.Copy).then_inc(qkg_kept, 1)
                else:
                    bank = PROJ_BANK[KINDS * th + kind]
                    nc.scalar.activation(to, PS[:, bank, 0:WIDTH].rearrange("p (t r) -> p r t", r=PATCH),
                                         ACT.Identity, bias=bias[:, kind:kind + 1]).then_inc(qkg_kept, 1)

            def keep_rest(n, at_end):
                for th in range(SIDE - 1):
                    for kind in range(KINDS):
                        if th or kind:
                            keep(n, th, kind, False)
                if isinstance(at_end, bool):
                    for kind in range(KINDS):
                        keep(n, SIDE - 1, kind, at_end)
                else:
                    with act.If(at_end):
                        for kind in range(KINDS):
                            keep(n, SIDE - 1, kind, True)
                    with act.Else():
                        for kind in range(KINDS):
                            keep(n, SIDE - 1, kind, False)

            def keep_pt(n, g):
                act.wait_ge(p_turned, GROUPS * n + g + 1)
                nc.scalar.activation(PT[:, g, :], PS[:, PT_BANK, g * TOK:(g + 1) * TOK], ACT.Copy).then_inc(p_kept, 1)

            def exponentials(n):
                for g in range(GROUPS):
                    act.wait_ge(maxed, GROUPS * n + g + 1)
                    nc.scalar.activation(E[:, g, :], S[:, g, :], ACT.Exp, bias=negmax[:, g:g + 1],
                                         accum_out=rowsum[:, g:g + 1]).then_inc(exped, 1)

            def strip(i, slot, last):
                n = i * SLOTS + slot
                more = not (last and slot == SLOTS - 1)
                act.wait_ge(g_turned, GROUPS * n + 1)
                nc.scalar.activation(GT[:, 0, :, :].rearrange("p r c -> p (r c)"),
                                     PS[:, WIDE_BANK[0]:WIDE_BANK[0] + 2, :].rearrange("p b c -> p (b c)"),
                                     ACT.Copy).then_inc(g0_kept, 1)
                keep_pt(n, 0)
                if more:
                    keep(n + 1, 0, Q, False)
                keep_pt(n, 1)
                for g in range(GROUPS):
                    act.wait_ge(mixed, GROUPS * n + g + 1)
                    b = WIDE_BANK[g]
                    for h in range(2):
                        lanes = slice(64 * h, 64 * h + 64)
                        nc.scalar.activation(o_place(lanes, h, g), o_bank(lanes, b), ACT.Copy).then_inc(o_high, 1)
                if more:
                    at_end = slot + 1 == SLOTS - 1
                    if at_end and not last:
                        at_end = i % PER_IMAGE == PER_IMAGE - 1
                    keep_rest(n + 1, at_end)
                    exponentials(n + 1)

            act.wait_ge(w_ready, 1)
            act.wait_ge(pads_made, 2 + 1 + KINDS)
            keep(0, 0, Q, False)
            keep_rest(0, False)
            exponentials(0)
            with act.Fori(0, PASSES - 1) as i:
                for slot in range(SLOTS):
                    strip(i, slot, False)
            for slot in range(SLOTS):
                strip(PASSES - 1, slot, True)

        @block.vector
        def _(dve):
            dve.wait_ge(small_loaded, 16 * 4)
            dve.wait_ge(pads_made, 2)
            for a in range(HALVES):
                nc.vector.tensor_copy(w_st[:, a, :, a], w_nat[:, :]).then_inc(w_stretched, 1)
                for m in range(2):
                    for h in range(2):
                        nc.vector.tensor_copy(wo_st[:, m, a, h, m, a, :], wo_nat[:, :]).then_inc(w_stretched, 1)
                nc.vector.tensor_copy(bo_st[:, :, a], bo_nat[:, :]).then_inc(w_stretched, 1)
            nc.vector.tensor_copy(b_st[:, :, :], b_nat[:, :].unsqueeze(1).broadcast_to([KINDS, HALVES * ROWS, C1])
                                  ).then_inc(w_stretched, 1)
            dve.wait_ge(w_turned, 1)
            nc.vector.tensor_copy(W[:, :, :].rearrange("p k (a o) -> p a k o", a=HALVES),
                                  PS[:, 0, 0:HALVES * KINDS * C1].rearrange("p (a k o) -> p a k o", a=HALVES, k=KINDS))
            nc.vector.tensor_copy(bias[:, :], PS[:, 4, 0:KINDS + 1]).then_inc(w_ready, 1)
            nc.vector.tensor_scalar(mask[:, :], PS[:, 4, 128:128 + NEAR], 1.0, BIG, ALU.subtract, ALU.mult)
            wo_ps = PS[:, 5, 0:2 * HALVES * CH].rearrange("p (m a c) -> p m a c", m=2, a=HALVES)
            nc.vector.tensor_copy(WOH[:, :, :, :].rearrange("p m c a -> p m a c"), wo_ps).then_inc(wo_high, 1)
            dve.wait_ge(wo_high, 1)
            nc.vector.tensor_tensor(WOL[:, :, :, :].rearrange("p m c a -> p m a c"), wo_ps,
                                    WOH[:, :, :, :].bitcast(fp32).rearrange("p m c a -> p m a c"),
                                    ALU.subtract).then_inc(wo_ready, 1)

            def mask_scores(n, g):
                dve.wait_ge(scored, GROUPS * n + g + 1)
                nc.vector.tensor_tensor(S[:, g, :], PS[:, SCORE_BANK[g], 0:NEAR], mask[:, :],
                                        ALU.add).then_inc(masked, 1)
                dve.wait_ge(masked, GROUPS * n + g + 1)
                nc.vector.tensor_reduce(negmax[:, g:g + 1], S[:, g, :], AX.X, ALU.max,
                                        negate=True).then_inc(maxed, 1)

            def norm(n, g):
                dve.wait_ge(exped, GROUPS * n + g + 1)
                nc.vector.reciprocal(inverse[:, g:g + 1], rowsum[:, g:g + 1]).then_inc(inverted, 1)
                dve.wait_ge(inverted, GROUPS * n + g + 1)
                for h in range(2):
                    half = slice(NEAR * h, NEAR * (h + 1))
                    nc.vector.tensor_scalar(P[half, g, half], E[half, g, :], inverse[half, g:g + 1], None,
                                            ALU.mult).then_inc(normed, 1)

            def add_x(n, slot, th, pair):
                dve.wait_ge(out_made, 2 * (SIDE * n + th) + pair + 1)
                b = OUT_BANK + 2 * pair
                rows = X[:, slot, th, 2 * pair:2 * pair + 2, :]
                nc.vector.scalar_tensor_tensor(
                    out=rows, in0=PS[:, b:b + 2, 0:WIDTH], scalar=bias[:, KINDS:KINDS + 1], in1=rows,
                    op0=ALU.add, op1=ALU.add).then_inc(out_kept, 1)

            def strip(i, slot, last):
                n = i * SLOTS + slot
                dve.wait_ge(g_turned, GROUPS * n + 2)
                nc.vector.tensor_copy(GT[:, 1, :, :].rearrange("p r c -> p (r c)"),
                                      PS[:, WIDE_BANK[1]:WIDE_BANK[1] + 2, :].rearrange("p b c -> p (b c)")
                                      ).then_inc(g1_kept, 1)
                for g in range(GROUPS):
                    b = WIDE_BANK[g]
                    for h in range(2):
                        dve.wait_ge(o_high, 2 * (GROUPS * n + g) + h + 1)
                        lanes = slice(64 * h, 64 * h + 64)
                        low = slice(64 - 64 * h, 128 - 64 * h)
                        nc.vector.tensor_tensor(o_place(low, h, g), o_bank(lanes, b),
                                                o_place(lanes, h, g).bitcast(fp32),
                                                ALU.subtract).then_inc(o_low, 1)
                for th in range(SIDE - 1):
                    for pair in range(2):
                        add_x(n, slot, th, pair)
                if not (last and slot == SLOTS - 1):
                    for g in range(GROUPS):
                        mask_scores(n + 1, g)
                    for g in range(GROUPS):
                        norm(n + 1, g)
                        add_x(n, slot, SIDE - 1, g)

            dve.wait_ge(pads_made, 2 + 1 + KINDS)
            for g in range(GROUPS):
                mask_scores(0, g)
            for g in range(GROUPS):
                norm(0, g)
            with dve.Fori(0, PASSES - 1) as i:
                for slot in range(SLOTS):
                    strip(i, slot, False)
            for slot in range(SLOTS):
                strip(PASSES - 1, slot, True)

        @block.tensor
        def _(pe):
            pe.wait_ge(consts_made, 2)
            pe.wait_ge(w_stretched, HALVES * 6 + 1)
            for a in range(HALVES):
                nc.tensor.transpose(PS[:, 0, a * KINDS * C1:(a + 1) * KINDS * C1],
                                    w_st[:, a, :, :].rearrange("k c a -> k (c a)"),
                                    ident[0:KINDS * C1, 0:KINDS * C1])
            for m in range(2):
                for a in range(HALVES):
                    j = m * HALVES + a
                    nc.tensor.transpose(PS[:, 5, j * CH:(j + 1) * CH],
                                        wo_st[:, m, a, :, :, :, :].rearrange("c h m a o -> c (h m a o)"),
                                        ident[0:CH, 0:CH])
            nc.tensor.matmul(PS[:, 4, 0:KINDS], b_st[:, :, :].rearrange("k j o -> k (j o)"), ident[0:KINDS, 0:KINDS],
                             start=True, stop=True)
            nc.tensor.matmul(PS[:, 4, KINDS:KINDS + 1], bo_st[:, :, :].rearrange("k c a -> k (c a)"), ident[0:1, 0:1],
                             start=True, stop=True)
            pattern = blocks4[:, :, :, :].rearrange("b h k t -> b (h k t)")
            nc.tensor.matmul(PS[:, 4, 128:128 + NEAR], pattern, pattern[:, 0:NEAR], start=True, stop=True).then_inc(w_turned, 1)
            pe.wait_ge(w_ready, 1)

            def project(i, n, slot, th, kinds):
                for kind in kinds:
                    j = KINDS * th + kind
                    if kind == Q:
                        pe.wait_ge(x_loaded[slot][th], 16 * (i + 1))
                    if j >= 4 and j not in (6, 7):
                        pe.wait_ge(qkg_kept, KINDS * SIDE * n + j - 3)
                    for r in range(ROWS):
                        lanes = slice(32 * r, 32 * r + 32)
                        mm = nc.tensor.matmul(PS[lanes, PROJ_BANK[j], 0:WIDTH], W[:, kind, :],
                                              X[:, slot, th, r, :], start=True, stop=True)
                    mm.then_inc(projected, 1)

            def score(n):
                pe.wait_ge(qkg_kept, KINDS * SIDE * (n + 1) - 1)
                for g in range(GROUPS):
                    for col in range(PATCH):
                        for h in range(2):
                            half = slice(NEAR * h, NEAR * (h + 1))
                            mm = nc.tensor.matmul(PS[half, SCORE_BANK[g], 0:NEAR], tokens(Q, col, g)[:, half],
                                                  tokens(K, col, g)[:, half],
                                                  start=(col == 0), stop=(col == PATCH - 1))
                    mm.then_inc(scored, 1)

            def turn_g(n, g):
                for col in range(PATCH):
                    c = col % 4
                    mm = nc.tensor.transpose(PS[:, WIDE_BANK[g] + col // 4, c * 128:(c + 1) * 128],
                                             tokens(G, col, g), ident[:, :])
                mm.then_inc(g_turned, 1)

            def turn_p(n, g):
                pe.wait_ge(normed, 2 * (GROUPS * n + g + 1))
                nc.tensor.transpose(PS[:, PT_BANK, g * TOK:(g + 1) * TOK], P[:, g, :], ident[:, :]).then_inc(p_turned, 1)

            def mix(g, cols):
                for col in cols:
                    c = col % 4
                    mm = nc.tensor.matmul(PS[:, WIDE_BANK[g] + col // 4, c * TOK:(c + 1) * TOK],
                                          GT[:, g, col, :], PT[:, g, :], start=True, stop=True)
                return mm

            def project_out(n, th, more):
                for pair in range(2):
                    if th:
                        pe.wait_ge(out_kept, 2 * (SIDE * n + th - 1) + pair + 1)
                    elif pair and more:
                        pe.wait_ge(qkg_kept, KINDS * SIDE * (n + 1) + 4)
                    for m in range(2):
                        for w in (WOH, WOL):
                            mm = nc.tensor.matmul(PS[:, OUT_BANK + 2 * pair + m, 0:WIDTH],
                                                  w[:, m, :, :].rearrange("p c a -> p (c a)"),
                                                  O[:, pair, th, 0:WIDTH], start=(w is WOH), stop=(w is WOL))
                    mm.then_inc(out_made, 1)

            def strip(i, slot, last):
                n = i * SLOTS + slot
                more = not (last and slot == SLOTS - 1)
                ahead = (i + (slot + 1) // SLOTS, n + 1, (slot + 1) % SLOTS)
                pe.wait_ge(qkg_kept, KINDS * SIDE * (n + 1))
                turn_g(n, 0)
                turn_p(n, 0)
                pe.wait_ge(normed, 2 * GROUPS * n + 3)
                turn_g(n, 1)
                if more:
                    project(*ahead, 0, (Q,))
                pe.wait_ge(g0_kept, n + 1)
                pe.wait_ge(p_kept, GROUPS * n + 1)
                mix(0, range(0, 4))
                turn_p(n, 1)
                mix(0, range(4, 8)).then_inc(mixed, 1)
                pe.wait_ge(g1_kept, n + 1)
                pe.wait_ge(p_kept, GROUPS * n + 2)
                mix(1, range(0, 8)).then_inc(mixed, 1)
                if more:
                    project(*ahead, 0, (K, G))
                    project(*ahead, 1, (Q, K, G))
                pe.wait_ge(o_high, 2 * GROUPS * (n + 1))
                pe.wait_ge(o_low, 2 * GROUPS * (n + 1))
                project_out(n, 0, more)
                if more:
                    project(*ahead, 2, (Q, K, G))
                project_out(n, 1, more)
                if more:
                    project(*ahead, 3, (Q, K, G))
                project_out(n, 2, more)
                if more:
                    score(n + 1)
                    project_out(n, 3, more)

            for th in range(SIDE):
                project(0, 0, 0, th, (Q, K, G))
            pe.wait_ge(wo_ready, 1)
            score(0)
            with pe.Fori(0, PASSES - 1) as i:
                for slot in range(SLOTS):
                    strip(i, slot, False)
            for slot in range(SLOTS):
                strip(PASSES - 1, slot, True)


_INS = ["x", "L0_conv_w_ptg", "L0_conv_b_ptg", "L0_conv_w_out", "L0_conv_b_out"]


def kernel(**inputs):
    import numpy as _np
    import concourse.bacc as _bacc
    from concourse import mybir as _mybir
    from concourse.bass_utils import run_bass_kernel_spmd as _run

    nc = _bacc.Bacc("TRN2", target_bir_lowering=False, num_devices=1)
    arrays, args = {}, []
    for name in _INS:
        a = _np.ascontiguousarray(inputs[name])
        arrays[f"in_{name}_dram"] = a
        args.append(nc.dram_tensor(f"in_{name}_dram", a.shape, _mybir.dt.from_np(a.dtype), kind="ExternalInput").ap())
    shape = tuple(inputs["x"].shape)
    args.append(nc.dram_tensor("out_0_dram", shape, _mybir.dt.float32, kind="ExternalOutput").ap())
    block_attention_kernel(nc, *args)
    r = _run(nc, [arrays], core_ids=[0])
    return r.results[0]["out_0_dram"]
```
